# Optimizing a Trainium2 kernel written in Bass

```python
import numpy as np
import jax
import jax.numpy as jnp

def _softmax(x, axis=-1):
    return jax.nn.softmax(x, axis=axis)

def _gelu(x):
    return jax.nn.gelu(x, approximate=True)

def _silu(x):
    return jax.nn.silu(x)

def _sigmoid(x):
    return jax.nn.sigmoid(x)

def _layernorm(x, axis=-1, eps=1e-05):
    m = jnp.mean(x, axis=axis, keepdims=True)
    v = jnp.var(x, axis=axis, keepdims=True)
    return (x - m) / jnp.sqrt(v + eps)

def _scatter_add(tgt, idx, src, axis=0):
    return tgt.at[idx].add(src)

def _segment_sum(src, seg, n):
    return jax.ops.segment_sum(src, seg, n)
kernel_name = 'mk_cond_seq_d1_seqx_r4_0da689'

def setup_inputs(seed: int=0):
    np.random.seed(seed)
    _w = jnp.asarray

    def _rec_inputs():
        import jax
        import jax.numpy as jnp
        _rk = jax.random.key(seed)
        x = -0.000125 + 0.9999 * jax.random.normal(jax.random.fold_in(_rk, 1), (16, 256, 256), jnp.float32)
        _lenS = 256 - jax.random.randint(jax.random.fold_in(_rk, 7), (16,), 0, max(1, 256 // 4) + 1, jnp.int32)
        _lenS2 = 256 - jax.random.randint(jax.random.fold_in(_rk, 8), (16,), 0, max(1, 256 // 4) + 1, jnp.int32)
        condB_t = jax.random.uniform(jax.random.fold_in(_rk, 11), (16,), jnp.float32, 0.0, 0.983423)
        return (x, condB_t)
    x, condB_t = _rec_inputs()

    def _L0_cond_setup():
        import jax, jax.numpy as jnp
        import numpy as np
        import math
        B, S, D, E = (32, 256, 256, 128)

        def _layer_norm(x, gamma, beta, eps=1e-05):
            mean = jnp.mean(x, axis=(-2, -1), keepdims=True)
            var = jnp.mean(jnp.square(x - mean), axis=(-2, -1), keepdims=True)
            return (x - mean) * jax.lax.rsqrt(var + eps) * gamma + beta

        def _noise_encoding(t, channels):
            half = channels // 2
            freqs = jnp.exp(jnp.arange(half, dtype=jnp.float32) * (-math.log(10000.0) / (half - 1)))
            emb = 5000.0 * t[:, None] * freqs[None, :]
            return jnp.concatenate([jnp.sin(emb), jnp.cos(emb)], axis=1)
        key = jax.random.key(seed)
        ks = jax.random.split(key, 20)

        def lin(k, fan_in, shape):
            return jax.random.normal(k, shape, jnp.float32) / np.sqrt(fan_in)
        inp = {'x': jax.random.normal(ks[0], (B, S, D), jnp.float32), 't': jax.random.uniform(ks[1], (B,), jnp.float32), 'W1': lin(ks[2], E, (E, 4 * E)), 'b1': jnp.zeros((4 * E,), jnp.float32), 'W2': lin(ks[3], 4 * E, (4 * E, 4 * E)), 'b2': jnp.zeros((4 * E,), jnp.float32), 'Wsc': lin(ks[4], 4 * E, (4 * E, D)), 'bsc': jnp.zeros((D,), jnp.float32), 'Wsh': lin(ks[5], 4 * E, (4 * E, D)), 'bsh': jnp.zeros((D,), jnp.float32), 'gamma': jnp.ones((S, D), jnp.float32), 'beta': jnp.zeros((S, D), jnp.float32), 'W_in': lin(ks[6], D, (D, D)), 'b_in': jnp.zeros((D,), jnp.float32), 'W_out': lin(ks[7], D, (D, D)), 'b_out': jnp.zeros((D,), jnp.float32)}
        return inp
    _L0_cond_all = _L0_cond_setup()
    _L0_cond_in = {k: v for k, v in _L0_cond_all.items() if k in ('W1', 'b1', 'W2', 'b2', 'Wsc', 'bsc', 'Wsh', 'bsh', 'gamma', 'beta', 'W_in', 'b_in', 'W_out', 'b_out')}
    del _L0_cond_all
    return {'x': x, 'condB_t': condB_t, 'L0_cond_W1': _L0_cond_in['W1'], 'L0_cond_b1': _L0_cond_in['b1'], 'L0_cond_W2': _L0_cond_in['W2'], 'L0_cond_b2': _L0_cond_in['b2'], 'L0_cond_Wsc': _L0_cond_in['Wsc'], 'L0_cond_bsc': _L0_cond_in['bsc'], 'L0_cond_Wsh': _L0_cond_in['Wsh'], 'L0_cond_bsh': _L0_cond_in['bsh'], 'L0_cond_gamma': _L0_cond_in['gamma'], 'L0_cond_beta': _L0_cond_in['beta'], 'L0_cond_W_in': _L0_cond_in['W_in'], 'L0_cond_b_in': _L0_cond_in['b_in'], 'L0_cond_W_out': _L0_cond_in['W_out'], 'L0_cond_b_out': _L0_cond_in['b_out']}

def reference(x, condB_t, L0_cond_W1, L0_cond_b1, L0_cond_W2, L0_cond_b2, L0_cond_Wsc, L0_cond_bsc, L0_cond_Wsh, L0_cond_bsh, L0_cond_gamma, L0_cond_beta, L0_cond_W_in, L0_cond_b_in, L0_cond_W_out, L0_cond_b_out):
    import jax
    import jax.numpy as jnp

    def _L0_cond_ref(x, t, W1, b1, W2, b2, Wsc, bsc, Wsh, bsh, gamma, beta, W_in, b_in, W_out, b_out):
        import jax, jax.numpy as jnp
        import numpy as np
        import math
        B, S, D, E = (32, 256, 256, 128)

        def _layer_norm(x, gamma, beta, eps=1e-05):
            mean = jnp.mean(x, axis=(-2, -1), keepdims=True)
            var = jnp.mean(jnp.square(x - mean), axis=(-2, -1), keepdims=True)
            return (x - mean) * jax.lax.rsqrt(var + eps) * gamma + beta

        def _noise_encoding(t, channels):
            half = channels // 2
            freqs = jnp.exp(jnp.arange(half, dtype=jnp.float32) * (-math.log(10000.0) / (half - 1)))
            emb = 5000.0 * t[:, None] * freqs[None, :]
            return jnp.concatenate([jnp.sin(emb), jnp.cos(emb)], axis=1)
        h = _noise_encoding(t, E)
        h = jax.nn.silu(h @ W1 + b1)
        h = h @ W2 + b2
        scale = (h @ Wsc + bsc)[:, None, :]
        shift = (h @ Wsh + bsh)[:, None, :]
        out = jax.nn.silu(scale * _layer_norm(x, gamma, beta) + shift)
        out = out @ W_in + b_in
        out = jax.nn.silu(scale * _layer_norm(out, gamma, beta) + shift)
        out = out @ W_out + b_out
        return out + x
    x = _L0_cond_ref(x, condB_t, L0_cond_W1, L0_cond_b1, L0_cond_W2, L0_cond_b2, L0_cond_Wsc, L0_cond_bsc, L0_cond_Wsh, L0_cond_bsh, L0_cond_gamma, L0_cond_beta, L0_cond_W_in, L0_cond_b_in, L0_cond_W_out, L0_cond_b_out)
    return x

_drawn_inputs = setup_inputs


def setup_inputs(seed=0):
    import zlib

    import numpy as np

    out = dict(_drawn_inputs(seed))
    spreads = {'L0_cond_b1': (0.0, 0.1),
     'L0_cond_b2': (0.0, 0.1),
     'L0_cond_bsc': (0.0, 0.1),
     'L0_cond_bsh': (0.0, 0.1),
     'L0_cond_gamma': (1.0, 0.2),
     'L0_cond_beta': (0.0, 0.281),
     'L0_cond_b_in': (0.0, 0.1),
     'L0_cond_b_out': (0.0, 0.1)}
    factors = {}
    for name, (base, spread) in spreads.items():
        noise = np.random.default_rng([zlib.crc32(name.encode()), seed]).standard_normal(out[name].shape)
        drawn = base * np.exp(spread * noise) if base else spread * noise
        out[name] = jnp.asarray(drawn.astype(out[name].dtype))
    for name, factor in factors.items():
        out[name] = (out[name] * factor).astype(out[name].dtype)
    return out
```

```python
from contextlib import ExitStack
import math

import numpy as np

import concourse.bass as bass
from concourse import mybir

F32 = mybir.dt.float32
BF16 = mybir.dt.bfloat16
ALU = mybir.AluOpType
ACT = mybir.ActivationFunctionType
AX = mybir.AxisListType

P = 128
B, S, D = 16, 256, 256
E = 128
H = 4 * E
C = D // P
KH = H // P
BP = 2
NP = B // BP
EPS = 1e-5

TURN_1 = 6.25
TURN_2 = 17.0 / 512.0
TURN_3 = 2.0 * math.pi - TURN_1 - TURN_2
ROUND = 1.5 * 2.0 ** 23
PI_BELOW = 3.1415925

COL_B1, COL_B2, COL_BSC, COL_BSH, COL_BIN, COL_BOUT = 0, KH, 2 * KH, 2 * KH + C, 2 * KH + 2 * C, 2 * KH + 3 * C
N_BIAS = 2 * KH + 4 * C
COL_FREQ, COL_TURNS, COL_PHASE = 0, 1, 2


def build(nc, x, t, w1, w2, wsc, wsh, biases, gamma, beta, w_in, w_out, enc, out):
    with ExitStack() as ctx:
        def sb(name, shape, dt=F32):
            return ctx.enter_context(nc.sbuf_tensor(name, shape, dt))

        def sem(name):
            return ctx.enter_context(nc.semaphore(name))

        x_sb = sb("x_sb", [P, NP, C, BP, S])
        act1 = sb("act1", [P, NP, C, BP, S])
        act2 = sb("act2", [P, 2, C, BP, S])
        o_sb = sb("o_sb", [P, 2, C, BP, S])
        squares = sb("squares", [P, S], BF16)
        w1_sb = sb("w1_sb", [P, H])
        w2_sb = sb("w2_sb", [P, KH, H])
        wss_sb = sb("wss_sb", [P, KH, 2, D])
        win_sb = sb("win_sb", [P, C, D])
        wout_sb = sb("wout_sb", [P, C, D])
        gamma_sb = sb("gamma_sb", [P, C, S])
        beta_sb = sb("beta_sb", [P, C, S])
        bias_sb = sb("bias_sb", [P, N_BIAS])
        enc_sb = sb("enc_sb", [P, 3])
        t_sb = sb("t_sb", [P, B])
        mean_w = sb("mean_w", [P, P])
        rowsum_w = sb("rowsum_w", [P, C, P])
        wsum = sb("wsum", [P, C])
        minus_half = sb("minus_half", [P, BP])
        angle = sb("angle", [P, B])
        turns = sb("turns", [P, B])
        h0 = sb("h0", [P, B])
        h1 = sb("h1", [P, KH, B])
        h2 = sb("h2", [P, KH, B])
        cond = sb("cond", [P, 2, C, B])
        mean_b = sb("mean_b", [P, 1])
        b_in_c = sb("b_in_c", [P, C])
        bn = sb("bn", [P, NP, BP, 6])
        part = sb("part", [P, NP, BP, 2])
        dev = sb("dev", [P, NP, BP])
        dev2 = sb("dev2", [P, NP, BP])
        neg_m1 = sb("neg_m1", [P, NP, BP])
        var1 = sb("var1", [P, NP, BP])
        rstd1 = sb("rstd1", [P, NP, BP])
        rowsum = sb("rowsum", [P, NP, C, BP])
        shift2 = sb("shift2", [P, NP, C, BP])
        sumsq = sb("sumsq", [P, NP, C, BP])
        var2 = sb("var2", [P, NP, BP])
        rstd2 = sb("rstd2", [P, NP, BP])

        big = [ctx.enter_context(nc.psum_tensor(f"big{i}", [P, C, BP * S], F32)) for i in range(3)]
        stat1 = ctx.enter_context(nc.psum_tensor("stat1", [P, 512], F32))
        stat2 = ctx.enter_context(nc.psum_tensor("stat2", [P, 512], F32))

        t_in, enc_in, w1_in, bias_in, w2_in = sem("t_in"), sem("enc_in"), sem("w1_in"), sem("bias_in"), sem("w2_in")
        wsc_in, wsh_in, win_in, wout_in = sem("wsc_in"), sem("wsh_in"), sem("win_in"), sem("wout_in")
        gamma_in, beta_in = sem("gamma_in"), sem("beta_in")
        x_in = [sem(f"x_in{p}") for p in range(NP)]
        out_done = [sem(f"out_done{i}") for i in range(2)]

        enc_step = sem("enc_step")
        consts_set = sem("consts_set")
        h0_ready, h1_mm, h1_ready = sem("h0_ready"), sem("h1_mm"), sem("h1_ready")
        h2_mm, h2_ready, cond_mm, cond_ready = sem("h2_mm"), sem("h2_ready"), sem("cond_mm"), sem("cond_ready")
        wsum_ready, rowsum_w_ready = sem("wsum_ready"), sem("rowsum_w_ready")
        mean_b_mm, mean_b_ready, b_in_c_ready = sem("mean_b_mm"), sem("mean_b_ready"), sem("b_in_c_ready")

        bn_done, part_ready = sem("bn_done"), sem("part_ready")
        mean1_mm, dev_ready, dev2_ready = sem("mean1_mm"), sem("dev_ready"), sem("dev2_ready")
        negm1_ready, var1_mm, var1_ready = sem("negm1_ready"), sem("var1_mm"), sem("var1_ready")
        rstd1_ready, centred, scaled, z1_ready = sem("rstd1_ready"), sem("centred"), sem("scaled"), sem("z1_ready")
        act1_ready, mean2_mm, y_mm = sem("act1_ready"), sem("mean2_mm"), sem("y_mm")
        shift2_ready, squared, var2_mm, var2_ready = sem("shift2_ready"), sem("squared"), sem("var2_mm"), sem("var2_ready")
        rstd2_ready, weighted, z2_ready, act2_ready = sem("rstd2_ready"), sem("weighted"), sem("z2_ready"), sem("act2_ready")
        o_mm, o_ready = sem("o_mm"), sem("o_ready")

        def bias_col(col, k=0):
            return bias_sb[:, col + k:col + k + 1]

        def y_slot(p):
            return big[(0 if p == 0 else 2 * p - 1) % 3]

        def o_slot(p):
            return big[(2 * p + 2 if p < NP - 1 else 2 * p + 1) % 3]

        def y_wait_free(pe, p):
            if p == 2:
                pe.wait_ge(weighted, C * BP)
            elif p > 2:
                pe.wait_ge(o_ready, C * (p - 2))

        def o_wait_free(pe, p):
            if p < NP - 1:
                if p > 0:
                    pe.wait_ge(weighted, C * BP * (p + 1))
            else:
                pe.wait_ge(o_ready, C * (NP - 2))

        block = ctx.enter_context(nc.Block())

        @block.sync
        def _(sp):
            def load_x(p):
                sp.dma_start(x_sb[:, p], x[p]).then_inc(x_in[p], 16)

            sp.dma_start(t_sb[:], t.rearrange("(a b) -> a b", a=1).to_broadcast([P, B])).then_inc(t_in, 16)
            sp.dma_start(enc_sb[:], enc).then_inc(enc_in, 16)
            sp.dma_start(bias_sb[:], biases).then_inc(bias_in, 16)
            sp.dma_start(w1_sb[:], w1).then_inc(w1_in, 16)
            load_x(0)
            sp.dma_start(w2_sb[:], w2.rearrange("(k p) n -> p k n", p=P)).then_inc(w2_in, 16)
            sp.dma_start(gamma_sb[:], gamma).then_inc(gamma_in, 16)
            sp.dma_start(beta_sb[:], beta).then_inc(beta_in, 16)
            sp.dma_start(wss_sb[:, :, 0, :], wsc.rearrange("(k p) n -> p k n", p=P)).then_inc(wsc_in, 16)
            sp.dma_start(wss_sb[:, :, 1, :], wsh.rearrange("(k p) n -> p k n", p=P)).then_inc(wsh_in, 16)
            load_x(1)
            sp.dma_start(win_sb[:], w_in.rearrange("(k p) n -> p k n", p=P)).then_inc(win_in, 16)
            load_x(2)
            sp.dma_start(wout_sb[:], w_out.rearrange("(k p) n -> p k n", p=P)).then_inc(wout_in, 16)
            for p in range(3, NP):
                load_x(p)
            for p in range(NP):
                sp.wait_ge(o_ready, C * (p + 1))
                sp.dma_start(out[p], o_sb[:, p % 2]).then_inc(out_done[p % 2], 16)
            sp.wait_ge(out_done[0], 16 * (NP // 2))
            sp.wait_ge(out_done[1], 16 * (NP // 2))

        @block.gpsimd
        def _(pool):
            nc.gpsimd.memset(minus_half[:], -0.5)
            nc.gpsimd.memset(mean_w[:], 1.0 / P).then_inc(consts_set, 1)
            pool.wait_ge(consts_set, 1)

            def layer1_input(p):
                pool.wait_ge(var1_ready, p + 1)
                nc.gpsimd.tensor_tensor(rstd1[:, p], var1[:, p], minus_half[:], ALU.pow).then_inc(rstd1_ready, 1)
                pool.wait_ge(rstd1_ready, p + 1)
                pool.wait_ge(negm1_ready, p + 1)
                pool.wait_ge(x_in[p], 16)
                for b in range(BP):
                    nc.gpsimd.tensor_scalar(act1[:, p, :, b], x_sb[:, p, :, b], neg_m1[:, p, b:b + 1],
                                            rstd1[:, p, b:b + 1], ALU.add, ALU.mult).then_inc(centred, 1)
                if p == 0:
                    pool.wait_ge(gamma_in, 16)
                    pool.wait_ge(beta_in, 16)
                for b in range(BP):
                    pool.wait_ge(centred, BP * p + b + 1)
                    nc.gpsimd.tensor_tensor(act1[:, p, :, b], act1[:, p, :, b], gamma_sb[:], ALU.mult).then_inc(scaled, 1)
                for b in range(BP):
                    pool.wait_ge(scaled, BP * p + b + 1)
                    nc.gpsimd.tensor_tensor(act1[:, p, :, b], act1[:, p, :, b], beta_sb[:], ALU.add).then_inc(z1_ready, 1)

            def layer2_rstd(p):
                pool.wait_ge(var2_ready, p + 1)
                nc.gpsimd.tensor_tensor(rstd2[:, p], var2[:, p], minus_half[:], ALU.pow).then_inc(rstd2_ready, 1)

            for p in range(3):
                layer1_input(p)
            for p in range(NP):
                layer2_rstd(p)
                if p + 3 < NP:
                    layer1_input(p + 3)

        @block.scalar
        def _(act):
            act.wait_ge(enc_step, 8)
            nc.scalar.activation(h0[:], angle[:], ACT.Sin).then_inc(h0_ready, 1)
            act.wait_ge(h1_mm, 1)
            act.wait_ge(bias_in, 16)
            for k in range(KH):
                nc.scalar.activation(h1[:, k], big[0][:, 0, k * B:(k + 1) * B], ACT.Silu,
                                     bias=bias_col(COL_B1, k)).then_inc(h1_ready, 1)

            def modulated_silu(buf, p, b, c, **kw):
                i = BP * p + b
                return nc.scalar.activation(buf[:, c, b], buf[:, c, b], ACT.Silu, bias=cond[:, 1, c, i:i + 1],
                                            scale=cond[:, 0, c, i:i + 1], **kw)

            def activate1(p):
                for b in range(BP):
                    act.wait_ge(z1_ready, BP * p + b + 1)
                    for c in range(C):
                        modulated_silu(act1[:, p], p, b, c,
                                       accum_out=rowsum[:, p, c, b:b + 1]).then_inc(act1_ready, 1)

            def square2(p):
                act.wait_ge(shift2_ready, p + 1)
                for c in range(C):
                    act.wait_ge(y_mm, C * p + c + 1)
                    for b in range(BP):
                        if C * BP * p + BP * c + b:
                            act.wait_ge(squared, C * BP * p + BP * c + b)
                        nc.scalar.activation(squares[:], y_slot(p)[:, c, b * S:(b + 1) * S], ACT.Square,
                                             bias=shift2[:, p, c, b:b + 1],
                                             accum_out=sumsq[:, p, c, b:b + 1]).then_inc(squared, 1)

            def activate2(p):
                for b in range(BP):
                    act.wait_ge(z2_ready, BP * p + b + 1)
                    for c in range(C):
                        modulated_silu(act2[:, p % 2], p, b, c).then_inc(act2_ready, 1)

            act.wait_ge(cond_ready, 1)
            activate1(0)
            for p in range(NP):
                if p > 0:
                    activate2(p - 1)
                square2(p)
                if p + 1 < NP:
                    activate1(p + 1)
            activate2(NP - 1)

        @block.vector
        def _(dve):
            dve.wait_ge(t_in, 16)
            dve.wait_ge(enc_in, 16)
            nc.vector.tensor_scalar(angle[:], t_sb[:], 5000.0, enc_sb[:, COL_FREQ:COL_FREQ + 1],
                                    ALU.mult, ALU.mult).then_inc(enc_step, 1)
            dve.wait_ge(enc_step, 1)
            nc.vector.tensor_scalar(turns[:], angle[:], 1.0 / (2.0 * math.pi), enc_sb[:, COL_TURNS:COL_TURNS + 1],
                                    ALU.mult, ALU.add).then_inc(enc_step, 1)
            dve.wait_ge(enc_step, 2)
            nc.vector.tensor_scalar(turns[:], turns[:], ROUND, -ROUND, ALU.add, ALU.add).then_inc(enc_step, 1)
            for n, part_of_turn in enumerate((TURN_1, TURN_2, TURN_3)):
                dve.wait_ge(enc_step, 3 + n)
                nc.vector.scalar_tensor_tensor(angle[:], turns[:], -part_of_turn, angle[:],
                                               ALU.mult, ALU.add).then_inc(enc_step, 1)
            dve.wait_ge(enc_step, 6)
            nc.vector.tensor_scalar(angle[:], angle[:], enc_sb[:, COL_PHASE:COL_PHASE + 1], PI_BELOW,
                                    ALU.add, ALU.min).then_inc(enc_step, 1)
            dve.wait_ge(enc_step, 7)
            nc.vector.tensor_scalar(angle[:], angle[:], -PI_BELOW, None, ALU.max).then_inc(enc_step, 1)

            def stats1(p):
                dve.wait_ge(x_in[p], 16)
                for b in range(BP):
                    nc.vector.bn_stats(bn[:, p, b], x_sb[:, p, :, b]).then_inc(bn_done, 1)
                for b in range(BP):
                    dve.wait_ge(bn_done, BP * p + b + 1)
                    nc.vector.bn_aggr(part[:, p, b], bn[:, p, b]).then_inc(part_ready, 1)

            def stats1_deviation(p):
                dve.wait_ge(mean1_mm, p + 1)
                nc.vector.tensor_tensor(dev[:, p], part[:, p, :, 0], stat1[:, 0:BP], ALU.subtract).then_inc(dev_ready, 1)
                nc.vector.tensor_scalar(neg_m1[:, p], stat1[:, 0:BP], -1.0, None, ALU.mult).then_inc(negm1_ready, 1)
                dve.wait_ge(dev_ready, p + 1)
                nc.vector.tensor_tensor(dev2[:, p], dev[:, p], dev[:, p], ALU.mult).then_inc(dev2_ready, 1)

            def stats1_variance(p):
                dve.wait_ge(var1_mm, p + 1)
                nc.vector.tensor_scalar(var1[:, p], stat1[:, 0:BP], EPS, None, ALU.add).then_inc(var1_ready, 1)

            def mean_shift2(p):
                dve.wait_ge(mean2_mm, p + 1)
                nc.vector.tensor_tensor(shift2[:, p], b_in_c[:].unsqueeze(2).to_broadcast([P, C, BP]),
                                        stat2[:, 0:BP].unsqueeze(1).to_broadcast([P, C, BP]),
                                        ALU.subtract).then_inc(shift2_ready, 1)

            def variance2(p):
                dve.wait_ge(var2_mm, p + 1)
                nc.vector.tensor_scalar(var2[:, p], stat2[:, 0:BP], float(P) / (S * D), EPS,
                                        ALU.mult, ALU.add).then_inc(var2_ready, 1)

            def weight2(p):
                dve.wait_ge(squared, C * BP * (p + 1))
                if p >= 2:
                    dve.wait_ge(o_mm, C * (p - 1))
                for c in range(C):
                    for b in range(BP):
                        nc.vector.scalar_tensor_tensor(act2[:, p % 2, c, b], y_slot(p)[:, c, b * S:(b + 1) * S],
                                                       shift2[:, p, c, b:b + 1], gamma_sb[:, c],
                                                       ALU.add, ALU.mult).then_inc(weighted, 1)

            def normalise2(p):
                dve.wait_ge(rstd2_ready, p + 1)
                dve.wait_ge(weighted, C * BP * (p + 1))
                for b in range(BP):
                    nc.vector.scalar_tensor_tensor(act2[:, p % 2, :, b], act2[:, p % 2, :, b], rstd2[:, p, b:b + 1],
                                                   beta_sb[:], ALU.mult, ALU.add).then_inc(z2_ready, 1)

            def finish(p):
                if p >= 2:
                    dve.wait_ge(out_done[p % 2], 16 * (p // 2))
                for c in range(C):
                    dve.wait_ge(o_mm, C * p + c + 1)
                    nc.vector.scalar_tensor_tensor(o_sb[:, p % 2, c].rearrange("q b s -> q (b s)"), o_slot(p)[:, c],
                                                   bias_col(COL_BOUT, c),
                                                   x_sb[:, p, c].rearrange("q b s -> q (b s)"),
                                                   ALU.add, ALU.add).then_inc(o_ready, 1)

            stats1(0)
            stats1_deviation(0)
            stats1_variance(0)
            dve.wait_ge(bias_in, 16)
            dve.wait_ge(h2_mm, 1)
            nc.vector.tensor_tensor(h2[:], big[1][:, 0, 0:KH * B].rearrange("p (k b) -> p k b", k=KH),
                                    bias_sb[:, COL_B2:COL_B2 + KH].unsqueeze(2).to_broadcast([P, KH, B]),
                                    ALU.add).then_inc(h2_ready, 1)
            stats1(1)
            stats1_deviation(1)
            stats1_variance(1)
            dve.wait_ge(cond_mm, 1)
            nc.vector.tensor_tensor(cond[:].rearrange("p a c b -> p (a c) b"),
                                    big[2][:, 0, 0:2 * C * B].rearrange("p (k b) -> p k b", k=2 * C),
                                    bias_sb[:, COL_BSC:COL_BSC + 2 * C].unsqueeze(2).to_broadcast([P, 2 * C, B]),
                                    ALU.add).then_inc(cond_ready, 1)
            dve.wait_ge(win_in, 16)
            nc.vector.tensor_reduce(wsum[:], win_sb[:], AX.X, ALU.add).then_inc(wsum_ready, 1)
            dve.wait_ge(wsum_ready, 1)
            dve.wait_ge(consts_set, 1)
            for k in range(C):
                nc.vector.tensor_scalar(rowsum_w[:, k], mean_w[:], wsum[:, k:k + 1], float(P) / (S * D),
                                        ALU.mult, ALU.mult).then_inc(rowsum_w_ready, 1)
            dve.wait_ge(mean_b_mm, 1)
            nc.vector.tensor_scalar(mean_b[:], stat2[:, 0:1], 1.0 / C, None, ALU.mult).then_inc(mean_b_ready, 1)
            dve.wait_ge(mean_b_ready, 1)
            nc.vector.tensor_scalar(b_in_c[:], bias_sb[:, COL_BIN:COL_BIN + C], mean_b[:, 0:1], None,
                                    ALU.subtract).then_inc(b_in_c_ready, 1)
            dve.wait_ge(b_in_c_ready, 1)
            stats1(2)
            stats1_deviation(2)
            stats1_variance(2)
            for p in range(NP):
                mean_shift2(p)
                weight2(p)
                if p + 3 < NP:
                    stats1(p + 3)
                    stats1_deviation(p + 3)
                variance2(p)
                if p + 3 < NP:
                    stats1_variance(p + 3)
                normalise2(p)
                if p > 0:
                    finish(p - 1)
            finish(NP - 1)

        @block.tensor
        def _(pe):
            def mean1(p):
                if p > 0:
                    pe.wait_ge(var1_ready, p)
                pe.wait_ge(part_ready, BP * (p + 1))
                nc.tensor.matmul(stat1[:, 0:BP], mean_w[:], part[:, p, :, 0], start=True, stop=True).then_inc(mean1_mm, 1)

            def variance1(p):
                pe.wait_ge(negm1_ready, p + 1)
                pe.wait_ge(dev2_ready, p + 1)
                nc.tensor.matmul(stat1[:, 0:BP], mean_w[:], part[:, p, :, 1], start=True, stop=False)
                nc.tensor.matmul(stat1[:, 0:BP], mean_w[:], dev2[:, p], start=False, stop=True).then_inc(var1_mm, 1)

            def product(acc, w, act_in, c):
                for k in range(C):
                    mm = nc.tensor.matmul(acc[:, c], w[:, k, c * P:(c + 1) * P],
                                          act_in[:, k].rearrange("p b s -> p (b s)"),
                                          start=(k == 0), stop=(k == C - 1))
                return mm

            def layer1(p):
                y_wait_free(pe, p)
                pe.wait_ge(act1_ready, C * BP * (p + 1))
                if p == 0:
                    pe.wait_ge(win_in, 16)
                    pe.wait_ge(cond_ready, 1)
                product(y_slot(p), win_sb, act1[:, p], 0).then_inc(y_mm, 1)
                if p == 0:
                    pe.wait_ge(rowsum_w_ready, C)
                    pe.wait_ge(mean_b_ready, 1)
                else:
                    pe.wait_ge(var2_ready, p)
                for k in range(C):
                    mm = nc.tensor.matmul(stat2[:, 0:BP], rowsum_w[:, k], rowsum[:, p, k], start=(k == 0), stop=(k == C - 1))
                mm.then_inc(mean2_mm, 1)
                product(y_slot(p), win_sb, act1[:, p], 1).then_inc(y_mm, 1)

            def variance2(p):
                pe.wait_ge(shift2_ready, p + 1)
                pe.wait_ge(squared, C * BP * (p + 1))
                for c in range(C):
                    mm = nc.tensor.matmul(stat2[:, 0:BP], mean_w[:], sumsq[:, p, c], start=(c == 0), stop=(c == C - 1))
                mm.then_inc(var2_mm, 1)

            def layer2(p, c):
                if c == 0:
                    o_wait_free(pe, p)
                    pe.wait_ge(act2_ready, C * BP * (p + 1))
                    if p == 0:
                        pe.wait_ge(wout_in, 16)
                product(o_slot(p), wout_sb, act2[:, p % 2], c).then_inc(o_mm, 1)

            pe.wait_ge(h0_ready, 1)
            pe.wait_ge(w1_in, 16)
            for n in range(KH):
                mm = nc.tensor.matmul(big[0][:, 0, n * B:(n + 1) * B], w1_sb[:, n * P:(n + 1) * P], h0[:], start=True, stop=True)
            mm.then_inc(h1_mm, 1)
            pe.wait_ge(consts_set, 1)
            mean1(0)
            variance1(0)
            pe.wait_ge(h1_ready, KH)
            pe.wait_ge(w2_in, 16)
            for n in range(KH):
                for k in range(KH):
                    mm = nc.tensor.matmul(big[1][:, 0, n * B:(n + 1) * B], w2_sb[:, k, n * P:(n + 1) * P], h1[:, k],
                                          start=(k == 0), stop=(k == KH - 1))
            mm.then_inc(h2_mm, 1)
            pe.wait_ge(bias_in, 16)
            for c in range(C):
                mm = nc.tensor.matmul(stat2[:, 0:1], mean_w[:], bias_col(COL_BIN, c), start=(c == 0), stop=(c == C - 1))
            mm.then_inc(mean_b_mm, 1)
            mean1(1)
            variance1(1)
            pe.wait_ge(h2_ready, 1)
            pe.wait_ge(wsc_in, 16)
            pe.wait_ge(wsh_in, 16)
            for n in range(2 * C):
                for k in range(KH):
                    mm = nc.tensor.matmul(big[2][:, 0, n * B:(n + 1) * B], wss_sb[:, k, n // C, (n % C) * P:(n % C + 1) * P],
                                          h2[:, k], start=(k == 0), stop=(k == KH - 1))
            mm.then_inc(cond_mm, 1)
            mean1(2)
            variance1(2)
            for p in range(NP):
                layer1(p)
                if p > 0:
                    layer2(p - 1, 0)
                variance2(p)
                if p + 3 < NP:
                    mean1(p + 3)
                if p > 0:
                    layer2(p - 1, 1)
                if p + 3 < NP:
                    variance1(p + 3)
            layer2(NP - 1, 0)
            layer2(NP - 1, 1)


def kernel(x, condB_t, L0_cond_W1, L0_cond_b1, L0_cond_W2, L0_cond_b2, L0_cond_Wsc, L0_cond_bsc, L0_cond_Wsh,
           L0_cond_bsh, L0_cond_gamma, L0_cond_beta, L0_cond_W_in, L0_cond_b_in, L0_cond_W_out, L0_cond_b_out):
    import concourse.bacc as bacc
    from concourse.bass_utils import run_bass_kernel_spmd

    def cols(a):
        return np.asarray(a).reshape(-1, P).T

    def features_first(a):
        return np.ascontiguousarray(np.asarray(a).T.reshape(C, P, S).transpose(1, 0, 2))

    half = E // 2
    freqs = np.exp(np.arange(half, dtype=np.float32) * np.float32(-math.log(10000.0) / (half - 1)))
    enc = np.zeros((P, 3), np.float32)
    enc[:, COL_FREQ] = np.tile(freqs, 2)
    enc[half:, COL_TURNS] = 0.25
    enc[half:, COL_PHASE] = math.pi / 2

    arrays = {
        "x": np.ascontiguousarray(np.asarray(x).reshape(NP, BP, S, C, P).transpose(0, 4, 3, 1, 2)),
        "t": np.ascontiguousarray(condB_t),
        "w1": np.ascontiguousarray(L0_cond_W1),
        "w2": np.ascontiguousarray(L0_cond_W2),
        "wsc": np.ascontiguousarray(L0_cond_Wsc),
        "wsh": np.ascontiguousarray(L0_cond_Wsh),
        "biases": np.ascontiguousarray(np.concatenate(
            [cols(a) for a in (L0_cond_b1, L0_cond_b2, L0_cond_bsc, L0_cond_bsh, L0_cond_b_in, L0_cond_b_out)], axis=1)),
        "gamma": features_first(L0_cond_gamma),
        "beta": features_first(L0_cond_beta),
        "w_in": np.ascontiguousarray(L0_cond_W_in),
        "w_out": np.ascontiguousarray(L0_cond_W_out),
        "enc": enc,
    }
    nc = bacc.Bacc("TRN2", target_bir_lowering=False, num_devices=1)
    args = {n: nc.dram_tensor(f"{n}_dram", a.shape, mybir.dt.from_np(a.dtype), kind="ExternalInput").ap()
            for n, a in arrays.items()}
    out = nc.dram_tensor("out_dram", (NP, P, C, BP, S), F32, kind="ExternalOutput").ap()
    build(nc, out=out, **args)
    r = run_bass_kernel_spmd(nc, [{f"{n}_dram": a for n, a in arrays.items()}], core_ids=[0])
    got = r.results[0]["out_dram"]
    return np.ascontiguousarray(got.transpose(0, 3, 4, 2, 1)).reshape(B, S, D)
```

```python
from contextlib import ExitStack
import math

import numpy as np

import concourse.bass as bass
from concourse import mybir

F32 = mybir.dt.float32
BF16 = mybir.dt.bfloat16
ALU = mybir.AluOpType
ACT = mybir.ActivationFunctionType
AX = mybir.AxisListType

P = 128
B, S, D = 16, 256, 256
E = 128
H = 4 * E
C = D // P
KH = H // P
BP = 2
NP = B // BP
EPS = 1e-5
GROUPS = ((0, 1), (1, 3), (3, 5), (5, NP))
N_WARM = 14

TURN_1 = 6.25
TURN_2 = 17.0 / 512.0
TURN_3 = 2.0 * math.pi - TURN_1 - TURN_2
ROUND = 1.5 * 2.0 ** 23
PI_BELOW = 3.1415925

COL_B1, COL_B2, COL_BSC, COL_BSH, COL_BIN, COL_BOUT = 0, KH, 2 * KH, 2 * KH + C, 2 * KH + 2 * C, 2 * KH + 3 * C
N_BIAS = 2 * KH + 4 * C
COL_FREQ, COL_TURNS, COL_PHASE = 0, 1, 2


def build(nc, x, t, w1, w2, wsc, wsh, biases, gamma, beta, w_in, w_out, enc, out):
    with ExitStack() as ctx:
        def sb(name, shape, dt=F32):
            return ctx.enter_context(nc.sbuf_tensor(name, shape, dt))

        def sem(name):
            return ctx.enter_context(nc.semaphore(name))

        x_sb = sb("x_sb", [P, NP, C, BP, S])
        act1 = sb("act1", [P, NP, C, BP, S])
        act2 = sb("act2", [P, 2, C, BP, S])
        o_sb = sb("o_sb", [P, 2, C, BP, S])
        squares = sb("squares", [P, S], BF16)
        w1_sb = sb("w1_sb", [P, H])
        w2_sb = sb("w2_sb", [P, KH, H])
        wss_sb = sb("wss_sb", [P, KH, 2, D])
        win_sb = sb("win_sb", [P, C, D])
        wout_sb = sb("wout_sb", [P, C, D])
        gamma_sb = sb("gamma_sb", [P, C, S])
        beta_sb = sb("beta_sb", [P, C, S])
        bias_sb = sb("bias_sb", [P, N_BIAS])
        enc_sb = sb("enc_sb", [P, 3])
        t_sb = sb("t_sb", [P, B])
        mean_w = sb("mean_w", [P, P])
        rowsum_w = sb("rowsum_w", [P, C, P])
        wsum = sb("wsum", [P, C])
        minus_half = sb("minus_half", [P, B])
        zeros = sb("zeros", [P, 512], BF16)
        angle = sb("angle", [P, B])
        turns = sb("turns", [P, B])
        h0 = sb("h0", [P, B])
        h1 = sb("h1", [P, KH, B])
        h2 = sb("h2", [P, KH, B])
        cond = sb("cond", [P, 2, C, B])
        mean_b = sb("mean_b", [P, 1])
        b_in_c = sb("b_in_c", [P, C])
        bn = sb("bn", [P, B, 6])
        part = sb("part", [P, B, 2])
        dev = sb("dev", [P, B])
        dev2 = sb("dev2", [P, B])
        neg_m1 = sb("neg_m1", [P, B])
        var1 = sb("var1", [P, B])
        rstd1 = sb("rstd1", [P, B])
        rowsum = sb("rowsum", [P, NP, C, BP])
        shift2 = sb("shift2", [P, NP, C, BP])
        sumsq = sb("sumsq", [P, NP, C, BP])
        var2 = sb("var2", [P, NP, BP])
        rstd2 = sb("rstd2", [P, NP, BP])

        big = [ctx.enter_context(nc.psum_tensor(f"big{i}", [P, C, BP * S], F32)) for i in range(3)]
        stat1 = ctx.enter_context(nc.psum_tensor("stat1", [P, 512], F32))
        stat2 = ctx.enter_context(nc.psum_tensor("stat2", [P, 512], F32))

        t_in, enc_in, w1_in, bias_in, w2_in = sem("t_in"), sem("enc_in"), sem("w1_in"), sem("bias_in"), sem("w2_in")
        wsc_in, wsh_in, win_in, wout_in = sem("wsc_in"), sem("wsh_in"), sem("win_in"), sem("wout_in")
        gamma_in, beta_in = sem("gamma_in"), sem("beta_in")
        x_in = [sem(f"x_in{p}") for p in range(NP)]
        out_done = [[sem(f"out_done{i}_{c}") for c in range(C)] for i in range(2)]

        enc_step = sem("enc_step")
        zeros_set, consts_set = sem("zeros_set"), sem("consts_set")
        h0_ready, h1_mm, h1_ready = sem("h0_ready"), sem("h1_mm"), sem("h1_ready")
        h2_mm, h2_ready, cond_mm, cond_ready = sem("h2_mm"), sem("h2_ready"), sem("cond_mm"), sem("cond_ready")
        wsum_ready, rowsum_w_ready = sem("wsum_ready"), sem("rowsum_w_ready")
        mean_b_mm, mean_b_ready, b_in_c_ready = sem("mean_b_mm"), sem("mean_b_ready"), sem("b_in_c_ready")

        bn_done, part_ready = sem("bn_done"), sem("part_ready")
        mean1_mm, dev_ready, dev2_ready = sem("mean1_mm"), sem("dev_ready"), sem("dev2_ready")
        negm1_ready, var1_mm, var1_ready = sem("negm1_ready"), sem("var1_mm"), sem("var1_ready")
        rstd1_ready, centred, scaled, z1_ready = sem("rstd1_ready"), sem("centred"), sem("scaled"), sem("z1_ready")
        scaled_first, z1_first_ready = sem("scaled_first"), sem("z1_first_ready")
        act1_ready, mean2_mm, y_mm = sem("act1_ready"), sem("mean2_mm"), sem("y_mm")
        shift2_ready, squared, var2_mm, var2_ready = sem("shift2_ready"), sem("squared"), sem("var2_mm"), sem("var2_ready")
        rstd2_ready, weighted, z2_ready, act2_ready = sem("rstd2_ready"), sem("weighted"), sem("z2_ready"), sem("act2_ready")
        o_mm, o_ready = sem("o_mm"), sem("o_ready")

        def bias_col(col, k=0):
            return bias_sb[:, col + k:col + k + 1]

        def y_slot(p):
            return big[(0 if p == 0 else 2 * p - 1) % 3]

        def o_slot(p):
            return big[(2 * p + 2 if p < NP - 1 else 2 * p + 1) % 3]

        def y_wait_free(pe, p):
            if p == 2:
                pe.wait_ge(weighted, C * BP)
            elif p > 2:
                pe.wait_ge(o_ready, C * (p - 2))

        def o_wait_free(pe, p):
            if p < NP - 1:
                if p > 0:
                    pe.wait_ge(weighted, C * BP * (p + 1))
            else:
                pe.wait_ge(o_ready, C * (NP - 2))

        block = ctx.enter_context(nc.Block())

        @block.sync
        def _(sp):
            def load_x(p):
                sp.dma_start(x_sb[:, p], x[p]).then_inc(x_in[p], 16)

            sp.dma_start(t_sb[:], t.rearrange("(a b) -> a b", a=1).to_broadcast([P, B])).then_inc(t_in, 16)
            sp.dma_start(enc_sb[:], enc).then_inc(enc_in, 16)
            sp.dma_start(bias_sb[:], biases).then_inc(bias_in, 16)
            sp.dma_start(w1_sb[:], w1).then_inc(w1_in, 16)
            sp.dma_start(w2_sb[:], w2.rearrange("(k p) n -> p k n", p=P)).then_inc(w2_in, 16)
            load_x(0)
            sp.dma_start(wss_sb[:, :, 0, :], wsc.rearrange("(k p) n -> p k n", p=P)).then_inc(wsc_in, 16)
            sp.dma_start(wss_sb[:, :, 1, :], wsh.rearrange("(k p) n -> p k n", p=P)).then_inc(wsh_in, 16)
            sp.dma_start(gamma_sb[:], gamma).then_inc(gamma_in, 16)
            sp.dma_start(beta_sb[:], beta).then_inc(beta_in, 16)
            load_x(1)
            sp.dma_start(win_sb[:], w_in.rearrange("(k p) n -> p k n", p=P)).then_inc(win_in, 16)
            load_x(2)
            load_x(3)
            sp.dma_start(wout_sb[:], w_out.rearrange("(k p) n -> p k n", p=P)).then_inc(wout_in, 16)
            for p in range(4, NP):
                load_x(p)
            for p in range(NP):
                for c in range(C):
                    sp.wait_ge(o_ready, C * p + c + 1)
                    sp.dma_start(out[p, :, c], o_sb[:, p % 2, c]).then_inc(out_done[p % 2][c], 16)
            for slot in out_done:
                for done in slot:
                    sp.wait_ge(done, 16 * (NP // 2))

        @block.gpsimd
        def _(pool):
            nc.gpsimd.memset(minus_half[:], -0.5)
            nc.gpsimd.memset(mean_w[:], 1.0 / P).then_inc(consts_set, 1)
            pool.wait_ge(consts_set, 1)

            def layer1_rstd(g):
                lo, hi = BP * GROUPS[g][0], BP * GROUPS[g][1]
                pool.wait_ge(var1_ready, g + 1)
                nc.gpsimd.tensor_tensor(rstd1[:, lo:hi], var1[:, lo:hi], minus_half[:, lo:hi], ALU.pow).then_inc(rstd1_ready, 1)

            def layer1_input(p):
                if p == 1:
                    pool.wait_ge(gamma_in, 16)
                    pool.wait_ge(beta_in, 16)
                for b in range(BP):
                    pool.wait_ge(centred, BP * p + b + 1)
                    nc.gpsimd.tensor_tensor(act1[:, p, :, b], act1[:, p, :, b], gamma_sb[:], ALU.mult).then_inc(scaled, 1)
                for b in range(BP):
                    pool.wait_ge(scaled, BP * (p - 1) + b + 1)
                    nc.gpsimd.tensor_tensor(act1[:, p, :, b], act1[:, p, :, b], beta_sb[:], ALU.add).then_inc(z1_ready, 1)

            def layer2_rstd(p):
                pool.wait_ge(var2_ready, p + 1)
                nc.gpsimd.tensor_tensor(rstd2[:, p], var2[:, p], minus_half[:, 0:BP], ALU.pow).then_inc(rstd2_ready, 1)

            layer1_rstd(0)
            layer1_rstd(1)
            layer1_input(1)
            layer1_input(2)
            for p in range(NP):
                layer2_rstd(p)
                if p < 2:
                    layer1_rstd(p + 2)
                if p + 3 < NP:
                    layer1_input(p + 3)

        @block.scalar
        def _(act):
            nc.scalar.preload_act_table_set("silu_and_others")
            act.wait_ge(enc_step, 8)
            nc.scalar.activation(h0[:], angle[:], ACT.Sin).then_inc(h0_ready, 1)
            act.wait_ge(h1_mm, 1)
            act.wait_ge(bias_in, 16)
            for k in range(KH):
                nc.scalar.activation(h1[:, k], big[0][:, 0, k * B:(k + 1) * B], ACT.Silu,
                                     bias=bias_col(COL_B1, k)).then_inc(h1_ready, 1)

            def modulated_silu(buf, p, b, c, **kw):
                i = BP * p + b
                return nc.scalar.activation(buf[:, c, b], buf[:, c, b], ACT.Silu, bias=cond[:, 1, c, i:i + 1],
                                            scale=cond[:, 0, c, i:i + 1], **kw)

            def activate1(p):
                if p == 0:
                    act.wait_ge(z1_first_ready, BP)
                else:
                    act.wait_ge(z1_ready, BP * p)
                for c in range(C):
                    for b in range(BP):
                        modulated_silu(act1[:, p], p, b, c,
                                       accum_out=rowsum[:, p, c, b:b + 1]).then_inc(act1_ready, 1)

            def square2(p):
                act.wait_ge(shift2_ready, p + 1)
                for c in range(C):
                    act.wait_ge(y_mm, C * p + c + 1)
                    for b in range(BP):
                        if C * BP * p + BP * c + b:
                            act.wait_ge(squared, C * BP * p + BP * c + b)
                        nc.scalar.activation(squares[:], y_slot(p)[:, c, b * S:(b + 1) * S], ACT.Square,
                                             bias=shift2[:, p, c, b:b + 1],
                                             accum_out=sumsq[:, p, c, b:b + 1]).then_inc(squared, 1)

            def activate2(p):
                for b in range(BP):
                    act.wait_ge(z2_ready, BP * p + b + 1)
                    for c in range(C):
                        modulated_silu(act2[:, p % 2], p, b, c).then_inc(act2_ready, 1)

            act.wait_ge(cond_ready, 1)
            activate1(0)
            for p in range(NP):
                if p > 0:
                    activate2(p - 1)
                square2(p)
                if p + 1 < NP:
                    activate1(p + 1)
            activate2(NP - 1)

        @block.vector
        def _(dve):
            nc.vector.memset(zeros[:], 0.0).then_inc(zeros_set, 1)
            dve.wait_ge(t_in, 16)
            dve.wait_ge(enc_in, 16)
            nc.vector.tensor_scalar(angle[:], t_sb[:], 5000.0, enc_sb[:, COL_FREQ:COL_FREQ + 1],
                                    ALU.mult, ALU.mult).then_inc(enc_step, 1)
            dve.wait_ge(enc_step, 1)
            nc.vector.tensor_scalar(turns[:], angle[:], 1.0 / (2.0 * math.pi), enc_sb[:, COL_TURNS:COL_TURNS + 1],
                                    ALU.mult, ALU.add).then_inc(enc_step, 1)
            dve.wait_ge(enc_step, 2)
            nc.vector.tensor_scalar(turns[:], turns[:], ROUND, -ROUND, ALU.add, ALU.add).then_inc(enc_step, 1)
            for n, part_of_turn in enumerate((TURN_1, TURN_2, TURN_3)):
                dve.wait_ge(enc_step, 3 + n)
                nc.vector.scalar_tensor_tensor(angle[:], turns[:], -part_of_turn, angle[:],
                                               ALU.mult, ALU.add).then_inc(enc_step, 1)
            dve.wait_ge(enc_step, 6)
            nc.vector.tensor_scalar(angle[:], angle[:], enc_sb[:, COL_PHASE:COL_PHASE + 1], PI_BELOW,
                                    ALU.add, ALU.min).then_inc(enc_step, 1)
            dve.wait_ge(enc_step, 7)
            nc.vector.tensor_scalar(angle[:], angle[:], -PI_BELOW, None, ALU.max).then_inc(enc_step, 1)

            def stats1(p):
                dve.wait_ge(x_in[p], 16)
                for b in range(BP * p, BP * (p + 1)):
                    nc.vector.bn_stats(bn[:, b], x_sb[:, p, :, b % BP]).then_inc(bn_done, 1)
                for b in range(BP * p, BP * (p + 1)):
                    dve.wait_ge(bn_done, b + 1)
                    nc.vector.bn_aggr(part[:, b], bn[:, b]).then_inc(part_ready, 1)

            def stats1_deviation(g):
                lo, hi = BP * GROUPS[g][0], BP * GROUPS[g][1]
                dve.wait_ge(mean1_mm, g + 1)
                nc.vector.tensor_tensor(dev[:, lo:hi], part[:, lo:hi, 0], stat1[:, lo:hi], ALU.subtract).then_inc(dev_ready, 1)
                nc.vector.tensor_scalar(neg_m1[:, lo:hi], stat1[:, lo:hi], -1.0, None, ALU.mult).then_inc(negm1_ready, 1)
                dve.wait_ge(dev_ready, g + 1)
                nc.vector.tensor_tensor(dev2[:, lo:hi], dev[:, lo:hi], dev[:, lo:hi], ALU.mult).then_inc(dev2_ready, 1)

            def stats1_variance(g):
                lo, hi = BP * GROUPS[g][0], BP * GROUPS[g][1]
                dve.wait_ge(var1_mm, g + 1)
                nc.vector.tensor_scalar(var1[:, lo:hi], stat1[:, lo:hi], EPS, None, ALU.add).then_inc(var1_ready, 1)

            def centre1(p):
                g = next(n for n, (lo, hi) in enumerate(GROUPS) if lo <= p < hi)
                dve.wait_ge(rstd1_ready, g + 1)
                dve.wait_ge(negm1_ready, g + 1)
                for b in range(BP):
                    i = BP * p + b
                    nc.vector.tensor_scalar(act1[:, p, :, b], x_sb[:, p, :, b], neg_m1[:, i:i + 1], rstd1[:, i:i + 1],
                                            ALU.add, ALU.mult).then_inc(centred, 1)

            def first_input():
                dve.wait_ge(gamma_in, 16)
                dve.wait_ge(beta_in, 16)
                for b in range(BP):
                    dve.wait_ge(centred, b + 1)
                    nc.vector.tensor_tensor(act1[:, 0, :, b], act1[:, 0, :, b], gamma_sb[:], ALU.mult).then_inc(scaled_first, 1)
                for b in range(BP):
                    dve.wait_ge(scaled_first, b + 1)
                    nc.vector.tensor_tensor(act1[:, 0, :, b], act1[:, 0, :, b], beta_sb[:], ALU.add).then_inc(z1_first_ready, 1)

            def mean_shift2(p):
                dve.wait_ge(mean2_mm, p + 1)
                nc.vector.tensor_tensor(shift2[:, p], b_in_c[:].unsqueeze(2).to_broadcast([P, C, BP]),
                                        stat2[:, 0:BP].unsqueeze(1).to_broadcast([P, C, BP]),
                                        ALU.subtract).then_inc(shift2_ready, 1)

            def variance2(p):
                dve.wait_ge(var2_mm, p + 1)
                nc.vector.tensor_scalar(var2[:, p], stat2[:, 0:BP], float(P) / (S * D), EPS,
                                        ALU.mult, ALU.add).then_inc(var2_ready, 1)

            def weight2(p):
                dve.wait_ge(squared, C * BP * (p + 1))
                if p >= 2:
                    dve.wait_ge(o_mm, C * (p - 1))
                for c in range(C):
                    for b in range(BP):
                        nc.vector.scalar_tensor_tensor(act2[:, p % 2, c, b], y_slot(p)[:, c, b * S:(b + 1) * S],
                                                       shift2[:, p, c, b:b + 1], gamma_sb[:, c],
                                                       ALU.add, ALU.mult).then_inc(weighted, 1)

            def normalise2(p):
                dve.wait_ge(rstd2_ready, p + 1)
                dve.wait_ge(weighted, C * BP * (p + 1))
                for b in range(BP):
                    nc.vector.scalar_tensor_tensor(act2[:, p % 2, :, b], act2[:, p % 2, :, b], rstd2[:, p, b:b + 1],
                                                   beta_sb[:], ALU.mult, ALU.add).then_inc(z2_ready, 1)

            def finish(p):
                for c in range(C):
                    if p >= 2:
                        dve.wait_ge(out_done[p % 2][c], 16 * (p // 2))
                    dve.wait_ge(o_mm, C * p + c + 1)
                    nc.vector.scalar_tensor_tensor(o_sb[:, p % 2, c].rearrange("q b s -> q (b s)"), o_slot(p)[:, c],
                                                   bias_col(COL_BOUT, c),
                                                   x_sb[:, p, c].rearrange("q b s -> q (b s)"),
                                                   ALU.add, ALU.add).then_inc(o_ready, 1)

            stats1(0)
            stats1_deviation(0)
            stats1_variance(0)
            dve.wait_ge(bias_in, 16)
            dve.wait_ge(h2_mm, 1)
            nc.vector.tensor_tensor(h2[:], big[1][:, 0, 0:KH * B].rearrange("p (k b) -> p k b", k=KH),
                                    bias_sb[:, COL_B2:COL_B2 + KH].unsqueeze(2).to_broadcast([P, KH, B]),
                                    ALU.add).then_inc(h2_ready, 1)
            centre1(0)
            first_input()
            dve.wait_ge(cond_mm, 1)
            nc.vector.tensor_tensor(cond[:].rearrange("p a c b -> p (a c) b"),
                                    big[2][:, 0, 0:2 * C * B].rearrange("p (k b) -> p k b", k=2 * C),
                                    bias_sb[:, COL_BSC:COL_BSC + 2 * C].unsqueeze(2).to_broadcast([P, 2 * C, B]),
                                    ALU.add).then_inc(cond_ready, 1)
            stats1(1)
            stats1(2)
            stats1_deviation(1)
            stats1_variance(1)
            dve.wait_ge(win_in, 16)
            nc.vector.tensor_reduce(wsum[:], win_sb[:], AX.X, ALU.add).then_inc(wsum_ready, 1)
            dve.wait_ge(mean_b_mm, 1)
            nc.vector.tensor_scalar(mean_b[:], stat2[:, 0:1], 1.0 / C, None, ALU.mult).then_inc(mean_b_ready, 1)
            dve.wait_ge(wsum_ready, 1)
            dve.wait_ge(consts_set, 1)
            for k in range(C):
                nc.vector.tensor_scalar(rowsum_w[:, k], mean_w[:], wsum[:, k:k + 1], float(P) / (S * D),
                                        ALU.mult, ALU.mult).then_inc(rowsum_w_ready, 1)
            dve.wait_ge(mean_b_ready, 1)
            nc.vector.tensor_scalar(b_in_c[:], bias_sb[:, COL_BIN:COL_BIN + C], mean_b[:, 0:1], None,
                                    ALU.subtract).then_inc(b_in_c_ready, 1)
            dve.wait_ge(b_in_c_ready, 1)
            centre1(1)
            centre1(2)
            mean_shift2(0)
            stats1(3)
            stats1(4)
            weight2(0)
            stats1_deviation(2)
            variance2(0)
            stats1_variance(2)
            normalise2(0)
            centre1(3)
            mean_shift2(1)
            centre1(4)
            stats1(5)
            stats1(6)
            weight2(1)
            stats1(7)
            stats1_deviation(3)
            variance2(1)
            stats1_variance(3)
            normalise2(1)
            finish(0)
            for p in range(2, NP):
                mean_shift2(p)
                if p + 3 < NP:
                    centre1(p + 3)
                weight2(p)
                variance2(p)
                normalise2(p)
                finish(p - 1)
            finish(NP - 1)

        @block.tensor
        def _(pe):
            def warm(n):
                for _ in range(n):
                    nc.tensor.matmul(big[2][:, 1], zeros[:, 0:P], zeros[:], start=True, stop=True)

            def mean1(g):
                lo, hi = BP * GROUPS[g][0], BP * GROUPS[g][1]
                if g > 0:
                    pe.wait_ge(var1_ready, g)
                pe.wait_ge(part_ready, hi)
                nc.tensor.matmul(stat1[:, lo:hi], mean_w[:], part[:, lo:hi, 0], start=True, stop=True).then_inc(mean1_mm, 1)

            def variance1(g):
                lo, hi = BP * GROUPS[g][0], BP * GROUPS[g][1]
                pe.wait_ge(negm1_ready, g + 1)
                pe.wait_ge(dev2_ready, g + 1)
                nc.tensor.matmul(stat1[:, lo:hi], mean_w[:], part[:, lo:hi, 1], start=True, stop=False)
                nc.tensor.matmul(stat1[:, lo:hi], mean_w[:], dev2[:, lo:hi], start=False, stop=True).then_inc(var1_mm, 1)

            def product(acc, w, act_in, c, chunk_wait=None):
                for k in range(C):
                    if chunk_wait is not None:
                        chunk_wait(k)
                    mm = nc.tensor.matmul(acc[:, c], w[:, k, c * P:(c + 1) * P],
                                          act_in[:, k].rearrange("p b s -> p (b s)"),
                                          start=(k == 0), stop=(k == C - 1))
                return mm

            def layer1(p):
                y_wait_free(pe, p)
                if p == 0:
                    pe.wait_ge(win_in, 16)
                    pe.wait_ge(cond_ready, 1)
                product(y_slot(p), win_sb, act1[:, p], 0,
                        lambda k: pe.wait_ge(act1_ready, C * BP * p + BP * (k + 1))).then_inc(y_mm, 1)
                if p == 0:
                    pe.wait_ge(rowsum_w_ready, C)
                    pe.wait_ge(mean_b_ready, 1)
                else:
                    pe.wait_ge(var2_ready, p)
                for k in range(C):
                    mm = nc.tensor.matmul(stat2[:, 0:BP], rowsum_w[:, k], rowsum[:, p, k], start=(k == 0), stop=(k == C - 1))
                mm.then_inc(mean2_mm, 1)
                product(y_slot(p), win_sb, act1[:, p], 1).then_inc(y_mm, 1)

            def variance2(p):
                pe.wait_ge(shift2_ready, p + 1)
                pe.wait_ge(squared, C * BP * (p + 1))
                for c in range(C):
                    mm = nc.tensor.matmul(stat2[:, 0:BP], mean_w[:], sumsq[:, p, c], start=(c == 0), stop=(c == C - 1))
                mm.then_inc(var2_mm, 1)

            def layer2(p, c):
                if c == 0:
                    o_wait_free(pe, p)
                    pe.wait_ge(act2_ready, C * BP * (p + 1))
                    if p == 0:
                        pe.wait_ge(wout_in, 16)
                product(o_slot(p), wout_sb, act2[:, p % 2], c).then_inc(o_mm, 1)

            pe.wait_ge(zeros_set, 1)
            warm(N_WARM)
            pe.wait_ge(h0_ready, 1)
            pe.wait_ge(w1_in, 16)
            for n in range(KH):
                mm = nc.tensor.matmul(big[0][:, 0, n * B:(n + 1) * B], w1_sb[:, n * P:(n + 1) * P], h0[:], start=True, stop=True)
            mm.then_inc(h1_mm, 1)
            warm(4)
            pe.wait_ge(h1_ready, KH)
            pe.wait_ge(w2_in, 16)
            pe.wait_ge(consts_set, 1)
            for n in range(KH):
                for k in range(KH):
                    mm = nc.tensor.matmul(big[1][:, 0, n * B:(n + 1) * B], w2_sb[:, k, n * P:(n + 1) * P], h1[:, k],
                                          start=(k == 0), stop=(k == KH - 1))
                if n == KH // 2:
                    mean1(0)
            mm.then_inc(h2_mm, 1)
            variance1(0)
            pe.wait_ge(bias_in, 16)
            for c in range(C):
                mm = nc.tensor.matmul(stat2[:, 0:1], mean_w[:], bias_col(COL_BIN, c), start=(c == 0), stop=(c == C - 1))
            mm.then_inc(mean_b_mm, 1)
            pe.wait_ge(h2_ready, 1)
            pe.wait_ge(wsc_in, 16)
            pe.wait_ge(wsh_in, 16)
            for n in range(2 * C):
                for k in range(KH):
                    mm = nc.tensor.matmul(big[2][:, 0, n * B:(n + 1) * B], wss_sb[:, k, n // C, (n % C) * P:(n % C + 1) * P],
                                          h2[:, k], start=(k == 0), stop=(k == KH - 1))
            mm.then_inc(cond_mm, 1)
            warm(4)
            mean1(1)
            variance1(1)
            for p in range(NP):
                layer1(p)
                if p > 0:
                    layer2(p - 1, 0)
                variance2(p)
                if p < 2:
                    mean1(p + 2)
                if p > 0:
                    layer2(p - 1, 1)
                if p < 2:
                    variance1(p + 2)
            layer2(NP - 1, 0)
            layer2(NP - 1, 1)


def kernel(x, condB_t, L0_cond_W1, L0_cond_b1, L0_cond_W2, L0_cond_b2, L0_cond_Wsc, L0_cond_bsc, L0_cond_Wsh,
           L0_cond_bsh, L0_cond_gamma, L0_cond_beta, L0_cond_W_in, L0_cond_b_in, L0_cond_W_out, L0_cond_b_out):
    import concourse.bacc as bacc
    from concourse.bass_utils import run_bass_kernel_spmd

    def cols(a):
        return np.asarray(a).reshape(-1, P).T

    def features_first(a):
        return np.ascontiguousarray(np.asarray(a).T.reshape(C, P, S).transpose(1, 0, 2))

    half = E // 2
    freqs = np.exp(np.arange(half, dtype=np.float32) * np.float32(-math.log(10000.0) / (half - 1)))
    enc = np.zeros((P, 3), np.float32)
    enc[:, COL_FREQ] = np.tile(freqs, 2)
    enc[half:, COL_TURNS] = 0.25
    enc[half:, COL_PHASE] = math.pi / 2

    arrays = {
        "x": np.ascontiguousarray(np.asarray(x).reshape(NP, BP, S, C, P).transpose(0, 4, 3, 1, 2)),
        "t": np.ascontiguousarray(condB_t),
        "w1": np.ascontiguousarray(L0_cond_W1),
        "w2": np.ascontiguousarray(L0_cond_W2),
        "wsc": np.ascontiguousarray(L0_cond_Wsc),
        "wsh": np.ascontiguousarray(L0_cond_Wsh),
        "biases": np.ascontiguousarray(np.concatenate(
            [cols(a) for a in (L0_cond_b1, L0_cond_b2, L0_cond_bsc, L0_cond_bsh, L0_cond_b_in, L0_cond_b_out)], axis=1)),
        "gamma": features_first(L0_cond_gamma),
        "beta": features_first(L0_cond_beta),
        "w_in": np.ascontiguousarray(L0_cond_W_in),
        "w_out": np.ascontiguousarray(L0_cond_W_out),
        "enc": enc,
    }
    nc = bacc.Bacc("TRN2", target_bir_lowering=False, num_devices=1)
    args = {n: nc.dram_tensor(f"{n}_dram", a.shape, mybir.dt.from_np(a.dtype), kind="ExternalInput").ap()
            for n, a in arrays.items()}
    out = nc.dram_tensor("out_dram", (NP, P, C, BP, S), F32, kind="ExternalOutput").ap()
    build(nc, out=out, **args)
    r = run_bass_kernel_spmd(nc, [{f"{n}_dram": a for n, a in arrays.items()}], core_ids=[0])
    got = r.results[0]["out_dram"]
    return np.ascontiguousarray(got.transpose(0, 3, 4, 2, 1)).reshape(B, S, D)
```

```python
from contextlib import ExitStack
import math

import numpy as np

import concourse.bass as bass
from concourse import mybir

F32 = mybir.dt.float32
BF16 = mybir.dt.bfloat16
ALU = mybir.AluOpType
ACT = mybir.ActivationFunctionType
AX = mybir.AxisListType

P = 128
B, S, D = 16, 256, 256
E = 128
H = 4 * E
C = D // P
KH = H // P
BP = 2
NP = B // BP
EPS = 1e-5
assert C == 2
GROUPS = ((0, 1), (1, 2), (2, 3), (3, 5), (5, 7), (7, NP))
CHAIN_OF_STEP = {1: 3, 3: 4, 5: 5}
N_WARM = 12

POOL_ONLY = (4, 5)
PRODUCTS = ["Y0", "Y1"] + [f"{layer}{p + 2 if layer == 'Y' else p}" for p in range(NP - 2) for layer in "YO"] + [f"O{NP - 2}", f"O{NP - 1}"]
ACCUMULATORS = 3
WARM_AFTER = 4
WARM_BETWEEN = 2

TURN_1 = 6.25
TURN_2 = 17.0 / 512.0
TURN_3 = 2.0 * math.pi - TURN_1 - TURN_2
ROUND = 1.5 * 2.0 ** 23
PI_BELOW = 3.1415925

COL_B1, COL_B2, COL_BSC, COL_BSH, COL_BIN, COL_BOUT = 0, KH, 2 * KH, 2 * KH + C, 2 * KH + 2 * C, 2 * KH + 3 * C
N_BIAS = 2 * KH + 4 * C
COL_FREQ, COL_TURNS, COL_PHASE, COL_EYE = 0, 1, 2, 3
N_ENC = COL_EYE + B


def build(nc, x, t, w1, w2, wsc, wsh, biases, gamma, beta, w_in, w_out, enc, out):
    with ExitStack() as ctx:
        def sb(name, shape, dt=F32):
            return ctx.enter_context(nc.sbuf_tensor(name, shape, dt))

        def sem(name):
            return ctx.enter_context(nc.semaphore(name))

        x_sb = sb("x_sb", [P, NP, C, BP, S])
        act1 = sb("act1", [P, NP, C, BP, S])
        act2 = sb("act2", [P, NP, C, BP, S])
        o_sb = sb("o_sb", [P, NP, C, BP, S])
        squares = sb("squares", [P, S], BF16)
        w1_sb = sb("w1_sb", [P, H])
        w2_sb = sb("w2_sb", [P, KH, H])
        wss_sb = sb("wss_sb", [P, KH, 2, D])
        win_sb = sb("win_sb", [P, C, D])
        wout_sb = sb("wout_sb", [P, C, D])
        gamma_sb = sb("gamma_sb", [P, C, S])
        beta_sb = sb("beta_sb", [P, C, S])
        bias_sb = sb("bias_sb", [P, N_BIAS])
        enc_sb = sb("enc_sb", [P, N_ENC])
        t_sb = sb("t_sb", [P, B])
        mean_w = sb("mean_w", [P, P])
        wsum = sb("wsum", [P, C])
        wmean = sb("wmean", [P, C])
        minus_half = sb("minus_half", [P, B])
        zeros = sb("zeros", [P, 512], BF16)
        angle = sb("angle", [P, B])
        turns = sb("turns", [P, B])
        h0 = sb("h0", [P, B])
        h1 = sb("h1", [P, KH, B])
        h2 = sb("h2", [P, KH, B])
        h2_rows = sb("h2_rows", [B, H])
        cond_rows = sb("cond_rows", [B, 2 * D])
        cond = sb("cond", [P, 2, C, B])
        mean_b = sb("mean_b", [P, 1])
        b_in_c = sb("b_in_c", [P, C])
        bn = sb("bn", [P, B, 6])
        part = sb("part", [P, B, 2])
        dev = sb("dev", [P, B])
        dev2 = sb("dev2", [P, B])
        neg_m1 = sb("neg_m1", [P, B])
        var1 = sb("var1", [P, B])
        rstd1 = sb("rstd1", [P, B])
        rowsum = sb("rowsum", [P, NP, C, BP])
        shift2 = sb("shift2", [P, NP, C, BP])
        wrow = sb("wrow", [P, NP, C, BP])
        wrow_sum = sb("wrow_sum", [P, NP, BP])
        sumsq = sb("sumsq", [P, NP, C, BP])
        sumsq_sum = sb("sumsq_sum", [P, NP, BP])
        var2 = sb("var2", [P, NP, BP])
        rstd2 = sb("rstd2", [P, NP, BP])

        big = [ctx.enter_context(nc.psum_tensor(f"big{i}", [P, C, BP * S], F32)) for i in range(ACCUMULATORS)]
        stat1 = ctx.enter_context(nc.psum_tensor("stat1", [P, 512], F32))
        stat2 = ctx.enter_context(nc.psum_tensor("stat2", [P, 512], F32))

        t_in, enc_in, w1_in, bias_in, w2_in = sem("t_in"), sem("enc_in"), sem("w1_in"), sem("bias_in"), sem("w2_in")
        wsc_in, wsh_in, win_in, wout_in = sem("wsc_in"), sem("wsh_in"), sem("win_in"), sem("wout_in")
        gamma_in, beta_in = sem("gamma_in"), sem("beta_in")
        x_in = [sem(f"x_in{p}") for p in range(NP)]
        out_done = sem("out_done")

        enc_step = sem("enc_step")
        zeros_set, consts_set = sem("zeros_set"), sem("consts_set")
        h0_ready, h1_mm, h1_ready = sem("h0_ready"), sem("h1_mm"), sem("h1_ready")
        h2_mm, h2_ready, cond_mm, cond_ready = sem("h2_mm"), sem("h2_ready"), sem("cond_mm"), sem("cond_ready")
        h2_rows_mm, h2_rows_ready = sem("h2_rows_mm"), sem("h2_rows_ready")
        cond_rows_mm, cond_rows_ready = sem("cond_rows_mm"), sem("cond_rows_ready")
        wsum_ready, wmean_ready = sem("wsum_ready"), sem("wmean_ready")
        mean_b_mm, mean_b_ready, b_in_c_ready = sem("mean_b_mm"), sem("mean_b_ready"), sem("b_in_c_ready")

        bn_done, part_ready = sem("bn_done"), sem("part_ready")
        mean1_mm, dev_ready, dev2_ready = sem("mean1_mm"), sem("dev_ready"), sem("dev2_ready")
        negm1_ready, var1_mm, var1_ready = sem("negm1_ready"), sem("var1_mm"), sem("var1_ready")
        rstd1_ready, centred, scaled, z1_ready = sem("rstd1_ready"), sem("centred"), sem("scaled"), sem("z1_ready")
        scaled_first, z1_first_ready = sem("scaled_first"), sem("z1_first_ready")
        act1_ready, mean2_mm, y_mm = sem("act1_ready"), sem("mean2_mm"), sem("y_mm")
        wrow_ready, wrow_sum_ready, sumsq_sum_ready = sem("wrow_ready"), sem("wrow_sum_ready"), sem("sumsq_sum_ready")
        shift2_ready, squared, var2_mm, var2_ready = sem("shift2_ready"), sem("squared"), sem("var2_mm"), sem("var2_ready")
        rstd2_ready, weighted, z2_ready, act2_ready = sem("rstd2_ready"), sem("weighted"), sem("z2_ready"), sem("act2_ready")
        o_mm, o_ready = sem("o_mm"), sem("o_ready")

        def bias_col(col, k=0):
            return bias_sb[:, col + k:col + k + 1]

        def pool_batches(p):
            return range(BP) if p in POOL_ONLY else range(1, BP)

        def pool_count(p):
            return sum(len(pool_batches(q)) for q in range(p))

        def dve_count(p):
            return BP * p - pool_count(p)

        def y_slot(p):
            return big[PRODUCTS.index(f"Y{p}") % ACCUMULATORS]

        def o_slot(p):
            return big[PRODUCTS.index(f"O{p}") % ACCUMULATORS]

        def wait_accumulator(pe, name):
            n = PRODUCTS.index(name)
            if n >= ACCUMULATORS:
                last = PRODUCTS[n - ACCUMULATORS]
                q = int(last[1:])
                if last[0] == "Y":
                    pe.wait_ge(weighted, C * BP * (q + 1))
                else:
                    pe.wait_ge(o_ready, C * (q + 1))

        pieces = [(p, c, b, n) for p in range(NP) for c in range(C)
                  for b, n in (((0, BP),) if (p, c) != (NP - 1, C - 1) else tuple((b, 1) for b in range(BP)))]

        def piece_slot(p, b, n):
            return o_slot(NP - 3) if (p, b, n) == (NP - 1, BP - 1, 1) else o_slot(p)

        block = ctx.enter_context(nc.Block())

        @block.sync
        def _(sp):
            def load_x(p):
                sp.dma_start(x_sb[:, p], x[p]).then_inc(x_in[p], 16)

            sp.dma_start(t_sb[:], t.rearrange("(a b) -> a b", a=1).to_broadcast([P, B])).then_inc(t_in, 16)
            sp.dma_start(enc_sb[:], enc).then_inc(enc_in, 16)
            sp.dma_start(bias_sb[:], biases).then_inc(bias_in, 16)
            sp.dma_start(w1_sb[:], w1).then_inc(w1_in, 16)
            sp.dma_start(w2_sb[:], w2.rearrange("(k p) n -> p k n", p=P)).then_inc(w2_in, 16)
            load_x(0)
            sp.dma_start(wss_sb[:, :, 0, :], wsc.rearrange("(k p) n -> p k n", p=P)).then_inc(wsc_in, 16)
            sp.dma_start(wss_sb[:, :, 1, :], wsh.rearrange("(k p) n -> p k n", p=P)).then_inc(wsh_in, 16)
            load_x(1)
            sp.dma_start(gamma_sb[:], gamma).then_inc(gamma_in, 16)
            sp.dma_start(beta_sb[:], beta).then_inc(beta_in, 16)
            sp.dma_start(win_sb[:], w_in.rearrange("(k p) n -> p k n", p=P)).then_inc(win_in, 16)
            load_x(2)
            load_x(3)
            sp.dma_start(wout_sb[:], w_out.rearrange("(k p) n -> p k n", p=P)).then_inc(wout_in, 16)
            for p in range(4, NP):
                load_x(p)
            for n_done, (p, c, b, n) in enumerate(pieces):
                sp.wait_ge(o_ready, n_done + 1)
                sp.dma_start(out[p, :, c, b:b + n], o_sb[:, p, c, b:b + n]).then_inc(out_done, 16)
            sp.wait_ge(out_done, 16 * len(pieces))

        @block.gpsimd
        def _(pool):
            nc.gpsimd.memset(minus_half[:], -0.5)
            nc.gpsimd.memset(mean_w[:], 1.0 / P).then_inc(consts_set, 1)
            pool.wait_ge(consts_set, 1)

            def layer1_rstd(g):
                lo, hi = BP * GROUPS[g][0], BP * GROUPS[g][1]
                pool.wait_ge(var1_ready, g + 1)
                nc.gpsimd.tensor_tensor(rstd1[:, lo:hi], var1[:, lo:hi], minus_half[:, lo:hi], ALU.pow).then_inc(rstd1_ready, 1)

            def layer1_input(p):
                if p == 0:
                    pool.wait_ge(gamma_in, 16)
                    pool.wait_ge(beta_in, 16)
                for n, b in enumerate(pool_batches(p)):
                    pool.wait_ge(centred, pool_count(p) + n + 1)
                    nc.gpsimd.tensor_tensor(act1[:, p, :, b], act1[:, p, :, b], gamma_sb[:], ALU.mult).then_inc(scaled, 1)
                for n, b in enumerate(pool_batches(p)):
                    pool.wait_ge(scaled, pool_count(p) + n + 1)
                    nc.gpsimd.tensor_tensor(act1[:, p, :, b], act1[:, p, :, b], beta_sb[:], ALU.add).then_inc(z1_ready, 1)

            def layer2_rstd(p):
                pool.wait_ge(var2_ready, p + 1)
                nc.gpsimd.tensor_tensor(rstd2[:, p], var2[:, p], minus_half[:, 0:BP], ALU.pow).then_inc(rstd2_ready, 1)

            for p in range(3):
                layer1_rstd(p)
                layer1_input(p)
            for p in range(NP):
                if CHAIN_OF_STEP.get(p + 1, 0) > 3:
                    layer1_rstd(CHAIN_OF_STEP[p + 1])
                layer2_rstd(p)
                if p == 0:
                    layer1_rstd(3)
                if p + 3 < NP:
                    layer1_input(p + 3)

        @block.scalar
        def _(act):
            nc.scalar.preload_act_table_set("silu_and_others")
            act.wait_ge(enc_step, 8)
            nc.scalar.activation(h0[:], angle[:], ACT.Sin).then_inc(h0_ready, 1)
            act.wait_ge(h1_mm, 1)
            act.wait_ge(bias_in, 16)
            for k in range(KH):
                nc.scalar.activation(h1[:, k], big[0][:, 0, k * B:(k + 1) * B], ACT.Silu,
                                     bias=bias_col(COL_B1, k)).then_inc(h1_ready, 1)

            def modulated_silu(buf, p, b, c, **kw):
                i = BP * p + b
                return nc.scalar.activation(buf[:, c, b], buf[:, c, b], ACT.Silu, bias=cond[:, 1, c, i:i + 1],
                                            scale=cond[:, 0, c, i:i + 1], **kw)

            def activate1(p):
                act.wait_ge(z1_ready, pool_count(p + 1))
                act.wait_ge(z1_first_ready, dve_count(p + 1))
                for c in range(C):
                    for b in range(BP):
                        modulated_silu(act1[:, p], p, b, c,
                                       accum_out=rowsum[:, p, c, b:b + 1]).then_inc(act1_ready, 1)

            def square2(p):
                act.wait_ge(shift2_ready, p + 1)
                for c in range(C):
                    act.wait_ge(y_mm, C * p + c + 1)
                    for b in range(BP):
                        if C * BP * p + BP * c + b:
                            act.wait_ge(squared, C * BP * p + BP * c + b)
                        nc.scalar.activation(squares[:], y_slot(p)[:, c, b * S:(b + 1) * S], ACT.Square,
                                             bias=shift2[:, p, c, b:b + 1],
                                             accum_out=sumsq[:, p, c, b:b + 1]).then_inc(squared, 1)

            def activate2(p):
                for c in range(C):
                    for b in range(BP):
                        act.wait_ge(z2_ready, BP * p + b + 1)
                        modulated_silu(act2[:, p], p, b, c).then_inc(act2_ready, 1)

            def copy_rows(rows, acc, rows_mm, rows_ready):
                act.wait_ge(rows_mm, 1)
                for i in range(2):
                    half = slice(i * H // 2, (i + 1) * H // 2)
                    nc.scalar.activation(rows[:, half], acc[0:B, 1, half], ACT.Identity).then_inc(rows_ready, 1)

            copy_rows(h2_rows, big[1], h2_rows_mm, h2_rows_ready)
            act.wait_ge(win_in, 16)
            for k in range(C):
                if k > 0:
                    act.wait_ge(wsum_ready, k)
                nc.scalar.activation(squares[:], win_sb[:, k], ACT.Identity, accum_out=wsum[:, k:k + 1]).then_inc(wsum_ready, 1)
            act.wait_ge(wsum_ready, C)
            copy_rows(cond_rows, big[2], cond_rows_mm, cond_rows_ready)
            act.wait_ge(cond_ready, 1)
            activate1(0)
            activate1(1)
            for p in range(NP):
                square2(p)
                if p > 0:
                    activate2(p - 1)
                if p + 2 < NP:
                    activate1(p + 2)
            activate2(NP - 1)

        @block.vector
        def _(dve):
            nc.vector.memset(zeros[:], 0.0).then_inc(zeros_set, 1)
            dve.wait_ge(t_in, 16)
            dve.wait_ge(enc_in, 16)
            nc.vector.tensor_scalar(angle[:], t_sb[:], 5000.0, enc_sb[:, COL_FREQ:COL_FREQ + 1],
                                    ALU.mult, ALU.mult).then_inc(enc_step, 1)
            dve.wait_ge(enc_step, 1)
            nc.vector.tensor_scalar(turns[:], angle[:], 1.0 / (2.0 * math.pi), enc_sb[:, COL_TURNS:COL_TURNS + 1],
                                    ALU.mult, ALU.add).then_inc(enc_step, 1)
            dve.wait_ge(enc_step, 2)
            nc.vector.tensor_scalar(turns[:], turns[:], ROUND, -ROUND, ALU.add, ALU.add).then_inc(enc_step, 1)
            for n, part_of_turn in enumerate((TURN_1, TURN_2, TURN_3)):
                dve.wait_ge(enc_step, 3 + n)
                nc.vector.scalar_tensor_tensor(angle[:], turns[:], -part_of_turn, angle[:],
                                               ALU.mult, ALU.add).then_inc(enc_step, 1)
            dve.wait_ge(enc_step, 6)
            nc.vector.tensor_scalar(angle[:], angle[:], enc_sb[:, COL_PHASE:COL_PHASE + 1], PI_BELOW,
                                    ALU.add, ALU.min).then_inc(enc_step, 1)
            dve.wait_ge(enc_step, 7)
            nc.vector.tensor_scalar(angle[:], angle[:], -PI_BELOW, None, ALU.max).then_inc(enc_step, 1)

            def stats1(p):
                dve.wait_ge(x_in[p], 16)
                for b in range(BP * p, BP * (p + 1)):
                    nc.vector.bn_stats(bn[:, b], x_sb[:, p, :, b % BP]).then_inc(bn_done, 1)
                for b in range(BP * p, BP * (p + 1)):
                    dve.wait_ge(bn_done, b + 1)
                    nc.vector.bn_aggr(part[:, b], bn[:, b]).then_inc(part_ready, 1)

            def stats1_deviation(g):
                lo, hi = BP * GROUPS[g][0], BP * GROUPS[g][1]
                dve.wait_ge(mean1_mm, g + 1)
                nc.vector.tensor_tensor(dev[:, lo:hi], part[:, lo:hi, 0], stat1[:, lo:hi], ALU.subtract).then_inc(dev_ready, 1)
                nc.vector.tensor_scalar(neg_m1[:, lo:hi], stat1[:, lo:hi], -1.0, None, ALU.mult).then_inc(negm1_ready, 1)
                dve.wait_ge(dev_ready, g + 1)
                nc.vector.tensor_tensor(dev2[:, lo:hi], dev[:, lo:hi], dev[:, lo:hi], ALU.mult).then_inc(dev2_ready, 1)

            def stats1_variance(g):
                lo, hi = BP * GROUPS[g][0], BP * GROUPS[g][1]
                dve.wait_ge(var1_mm, g + 1)
                nc.vector.tensor_scalar(var1[:, lo:hi], stat1[:, lo:hi], EPS, None, ALU.add).then_inc(var1_ready, 1)

            def group_of(p):
                return next(n for n, (lo, hi) in enumerate(GROUPS) if lo <= p < hi)

            def centre1(p):
                dve.wait_ge(rstd1_ready, group_of(p) + 1)
                dve.wait_ge(negm1_ready, group_of(p) + 1)
                for b in pool_batches(p):
                    i = BP * p + b
                    nc.vector.tensor_scalar(act1[:, p, :, b], x_sb[:, p, :, b], neg_m1[:, i:i + 1], rstd1[:, i:i + 1],
                                            ALU.add, ALU.mult).then_inc(centred, 1)

            def weigh_gamma(p):
                if p == 0:
                    dve.wait_ge(gamma_in, 16)
                dve.wait_ge(negm1_ready, group_of(p) + 1)
                nc.vector.scalar_tensor_tensor(act1[:, p, :, 0], x_sb[:, p, :, 0], neg_m1[:, BP * p:BP * p + 1], gamma_sb[:],
                                               ALU.add, ALU.mult).then_inc(scaled_first, 1)

            def weigh_beta(p):
                if p == 0:
                    dve.wait_ge(beta_in, 16)
                dve.wait_ge(rstd1_ready, group_of(p) + 1)
                dve.wait_ge(scaled_first, dve_count(p + 1))
                nc.vector.scalar_tensor_tensor(act1[:, p, :, 0], act1[:, p, :, 0], rstd1[:, BP * p:BP * p + 1], beta_sb[:],
                                               ALU.mult, ALU.add).then_inc(z1_first_ready, 1)

            def mean2_partial(p):
                dve.wait_ge(act1_ready, C * BP * (p + 1))
                nc.vector.tensor_tensor(wrow[:, p], rowsum[:, p], wmean[:].unsqueeze(2).to_broadcast([P, C, BP]),
                                        ALU.mult).then_inc(wrow_ready, 1)
                dve.wait_ge(wrow_ready, p + 1)
                nc.vector.tensor_tensor(wrow_sum[:, p], wrow[:, p, 0], wrow[:, p, 1], ALU.add).then_inc(wrow_sum_ready, 1)

            def mean_shift2(p):
                dve.wait_ge(mean2_mm, p + 1)
                nc.vector.tensor_tensor(shift2[:, p], b_in_c[:].unsqueeze(2).to_broadcast([P, C, BP]),
                                        stat2[:, 0:BP].unsqueeze(1).to_broadcast([P, C, BP]),
                                        ALU.subtract).then_inc(shift2_ready, 1)

            def variance2(p):
                dve.wait_ge(var2_mm, p + 1)
                nc.vector.tensor_scalar(var2[:, p], stat2[:, 0:BP], float(P) / (S * D), EPS,
                                        ALU.mult, ALU.add).then_inc(var2_ready, 1)

            def sum_squares2(p):
                dve.wait_ge(squared, C * BP * (p + 1))
                nc.vector.tensor_tensor(sumsq_sum[:, p], sumsq[:, p, 0], sumsq[:, p, 1], ALU.add).then_inc(sumsq_sum_ready, 1)

            def weight2(p):
                for c in range(C):
                    for b in range(BP):
                        nc.vector.scalar_tensor_tensor(act2[:, p, c, b], y_slot(p)[:, c, b * S:(b + 1) * S],
                                                       shift2[:, p, c, b:b + 1], gamma_sb[:, c],
                                                       ALU.add, ALU.mult).then_inc(weighted, 1)

            def normalise2(p):
                dve.wait_ge(rstd2_ready, p + 1)
                dve.wait_ge(weighted, C * BP * (p + 1))
                for b in range(BP):
                    nc.vector.scalar_tensor_tensor(act2[:, p, :, b], act2[:, p, :, b], rstd2[:, p, b:b + 1],
                                                   beta_sb[:], ALU.mult, ALU.add).then_inc(z2_ready, 1)

            def finish(p):
                for n_done, (q, c, b, n) in enumerate(pieces):
                    if q == p:
                        dve.wait_ge(o_mm, n_done + 1)
                        nc.vector.scalar_tensor_tensor(o_sb[:, p, c, b:b + n].rearrange("q b s -> q (b s)"),
                                                       piece_slot(p, b, n)[:, c, b * S:(b + n) * S], bias_col(COL_BOUT, c),
                                                       x_sb[:, p, c, b:b + n].rearrange("q b s -> q (b s)"),
                                                       ALU.add, ALU.add).then_inc(o_ready, 1)

            stats1(0)
            stats1_deviation(0)
            stats1_variance(0)
            dve.wait_ge(bias_in, 16)
            dve.wait_ge(h2_mm, 1)
            nc.vector.tensor_tensor(h2[:], big[1][:, 0, 0:KH * B].rearrange("p (k b) -> p k b", k=KH),
                                    bias_sb[:, COL_B2:COL_B2 + KH].unsqueeze(2).to_broadcast([P, KH, B]),
                                    ALU.add).then_inc(h2_ready, 1)
            centre1(0)
            stats1(1)
            stats1_deviation(1)
            weigh_gamma(0)
            weigh_beta(0)
            stats1_variance(1)
            stats1(2)
            dve.wait_ge(cond_mm, 1)
            nc.vector.tensor_tensor(cond[:].rearrange("p a c b -> p (a c) b"),
                                    big[2][:, 0, 0:2 * C * B].rearrange("p (k b) -> p k b", k=2 * C),
                                    bias_sb[:, COL_BSC:COL_BSC + 2 * C].unsqueeze(2).to_broadcast([P, 2 * C, B]),
                                    ALU.add).then_inc(cond_ready, 1)
            centre1(1)
            stats1_deviation(2)
            weigh_gamma(1)
            dve.wait_ge(mean_b_mm, 1)
            nc.vector.tensor_scalar(mean_b[:], stat2[:, 0:1], 1.0 / C, None, ALU.mult).then_inc(mean_b_ready, 1)
            dve.wait_ge(wsum_ready, C)
            nc.vector.tensor_scalar(wmean[:], wsum[:], float(P) / (S * D), None, ALU.mult).then_inc(wmean_ready, 1)
            dve.wait_ge(mean_b_ready, 1)
            nc.vector.tensor_scalar(b_in_c[:], bias_sb[:, COL_BIN:COL_BIN + C], mean_b[:, 0:1], None,
                                    ALU.subtract).then_inc(b_in_c_ready, 1)
            weigh_beta(1)
            stats1_variance(2)
            dve.wait_ge(wmean_ready, 1)
            dve.wait_ge(b_in_c_ready, 1)
            mean2_partial(0)
            stats1(3)
            mean_shift2(0)
            centre1(2)
            stats1(4)
            mean2_partial(1)
            weigh_gamma(2)
            weigh_beta(2)
            stats1_deviation(3)
            mean_shift2(1)
            sum_squares2(0)
            weight2(0)
            stats1_variance(3)
            variance2(0)
            mean2_partial(2)
            normalise2(0)
            centre1(3)
            mean_shift2(2)
            sum_squares2(1)
            stats1(5)
            weigh_gamma(3)
            weigh_beta(3)
            weight2(1)
            centre1(4)
            variance2(1)
            mean2_partial(3)
            stats1(6)
            normalise2(1)
            mean_shift2(3)
            stats1_deviation(4)
            sum_squares2(2)
            weight2(2)
            stats1_variance(4)
            variance2(2)
            finish(0)
            stats1(7)
            mean2_partial(4)
            centre1(5)
            sum_squares2(3)
            normalise2(2)
            mean_shift2(4)
            weight2(3)
            for p in range(4, NP):
                if p > 4:
                    mean_shift2(p)
                if CHAIN_OF_STEP.get(p):
                    stats1_deviation(CHAIN_OF_STEP[p])
                finish(p - 3)
                if CHAIN_OF_STEP.get(p):
                    stats1_variance(CHAIN_OF_STEP[p])
                variance2(p - 1)
                if p + 2 < NP:
                    centre1(p + 2)
                    if p + 2 not in POOL_ONLY:
                        weigh_gamma(p + 2)
                        weigh_beta(p + 2)
                if p + 1 < NP:
                    mean2_partial(p + 1)
                if p < NP - 1:
                    normalise2(p - 1)
                    sum_squares2(p)
                else:
                    sum_squares2(p)
                    normalise2(p - 1)
                    variance2(p)
                weight2(p)
            normalise2(NP - 1)
            finish(NP - 3)
            finish(NP - 2)
            finish(NP - 1)

        @block.tensor
        def _(pe):
            def warm(n):
                for _ in range(n):
                    nc.tensor.matmul(big[0][:, 1], zeros[:, 0:P], zeros[:], start=True, stop=True)

            def transposed(acc, rows, rows_ready):
                warm(WARM_BETWEEN)
                pe.wait_ge(enc_in, 16)
                for n in range(H // P):
                    pe.wait_ge(rows_ready, n // 2 + 1)
                    mm = nc.tensor.matmul(acc[:, 0, n * B:(n + 1) * B], rows[:, n * P:(n + 1) * P],
                                          enc_sb[0:B, COL_EYE:COL_EYE + B], start=True, stop=True)
                return mm

            def mean1(g):
                lo, hi = BP * GROUPS[g][0], BP * GROUPS[g][1]
                if g > 0:
                    pe.wait_ge(var1_ready, g)
                pe.wait_ge(part_ready, hi)
                nc.tensor.matmul(stat1[:, lo:hi], mean_w[:], part[:, lo:hi, 0], start=True, stop=True).then_inc(mean1_mm, 1)

            def variance1(g):
                lo, hi = BP * GROUPS[g][0], BP * GROUPS[g][1]
                pe.wait_ge(negm1_ready, g + 1)
                pe.wait_ge(dev2_ready, g + 1)
                nc.tensor.matmul(stat1[:, lo:hi], mean_w[:], part[:, lo:hi, 1], start=True, stop=False)
                nc.tensor.matmul(stat1[:, lo:hi], mean_w[:], dev2[:, lo:hi], start=False, stop=True).then_inc(var1_mm, 1)

            def product(acc, w, act_in, c, chunk_wait=None, batches=(0, BP)):
                b, n = batches
                for k in range(C):
                    if chunk_wait is not None:
                        chunk_wait(k)
                    mm = nc.tensor.matmul(acc[:, c, b * S:(b + n) * S], w[:, k, c * P:(c + 1) * P],
                                          act_in[:, k, b:b + n].rearrange("p b s -> p (b s)"),
                                          start=(k == 0), stop=(k == C - 1))
                return mm

            def mean2(p):
                pe.wait_ge(wrow_sum_ready, p + 1)
                if p == 0:
                    pe.wait_ge(mean_b_ready, 1)
                elif p == 1:
                    pe.wait_ge(shift2_ready, 1)
                else:
                    pe.wait_ge(var2_ready, p - 1)
                nc.tensor.matmul(stat2[:, 0:BP], mean_w[:], wrow_sum[:, p], start=True, stop=True).then_inc(mean2_mm, 1)

            def variance2(p):
                if p < NP - 1:
                    pe.wait_ge(shift2_ready, p + 2)
                else:
                    pe.wait_ge(var2_ready, p)
                pe.wait_ge(sumsq_sum_ready, p + 1)
                nc.tensor.matmul(stat2[:, 0:BP], mean_w[:], sumsq_sum[:, p], start=True, stop=True).then_inc(var2_mm, 1)

            def layer2(p, c):
                if c == 0:
                    wait_accumulator(pe, f"O{p}")
                    if p == 0:
                        pe.wait_ge(wout_in, 16)
                for q, c_piece, b, n in pieces:
                    if (q, c_piece) == (p, c):
                        if piece_slot(p, b, n) is not o_slot(p):
                            pe.wait_ge(o_ready, C * (NP - 2))
                        product(piece_slot(p, b, n), wout_sb, act2[:, p], c,
                                lambda k: pe.wait_ge(act2_ready, C * BP * p + BP * (k + 1)), batches=(b, n)).then_inc(o_mm, 1)

            pe.wait_ge(zeros_set, 1)
            warm(N_WARM)
            pe.wait_ge(h0_ready, 1)
            pe.wait_ge(w1_in, 16)
            for n in range(KH):
                mm = nc.tensor.matmul(big[0][:, 0, n * B:(n + 1) * B], w1_sb[:, n * P:(n + 1) * P], h0[:], start=True, stop=True)
            mm.then_inc(h1_mm, 1)
            warm(4)
            pe.wait_ge(h1_ready, KH)
            pe.wait_ge(w2_in, 16)
            pe.wait_ge(consts_set, 1)
            for k in range(KH):
                mm = nc.tensor.matmul(big[1][0:B, 1], h1[:, k], w2_sb[:, k], start=(k == 0), stop=(k == KH - 1))
                if k == KH - 1:
                    mm.then_inc(h2_rows_mm, 1)
                if k == 2:
                    mean1(0)
            variance1(0)
            transposed(big[1], h2_rows, h2_rows_ready).then_inc(h2_mm, 1)
            pe.wait_ge(bias_in, 16)
            for c in range(C):
                mm = nc.tensor.matmul(stat2[:, 0:1], mean_w[:], bias_col(COL_BIN, c), start=(c == 0), stop=(c == C - 1))
            mm.then_inc(mean_b_mm, 1)
            pe.wait_ge(h2_ready, 1)
            pe.wait_ge(wsc_in, 16)
            pe.wait_ge(wsh_in, 16)
            for k in range(KH):
                mm = nc.tensor.matmul(big[2][0:B, 1], h2[:, k], wss_sb[:, k].rearrange("p a n -> p (a n)"),
                                      start=(k == 0), stop=(k == KH - 1))
                if k == KH - 1:
                    mm.then_inc(cond_rows_mm, 1)
                if k == 1:
                    mean1(1)
            variance1(1)
            transposed(big[2], cond_rows, cond_rows_ready).then_inc(cond_mm, 1)
            mean1(2)
            warm(WARM_AFTER)
            variance1(2)
            pe.wait_ge(win_in, 16)
            pe.wait_ge(cond_ready, 1)
            for p in range(NP):
                wait_accumulator(pe, f"Y{p}")
                product(y_slot(p), win_sb, act1[:, p], 0,
                        lambda k: pe.wait_ge(act1_ready, C * BP * p + BP * (k + 1))).then_inc(y_mm, 1)
                if CHAIN_OF_STEP.get(p):
                    mean1(CHAIN_OF_STEP[p])
                mean2(p)
                product(y_slot(p), win_sb, act1[:, p], 1).then_inc(y_mm, 1)
                if CHAIN_OF_STEP.get(p):
                    variance1(CHAIN_OF_STEP[p])
                if p > 0:
                    variance2(p - 1)
                if p >= 2:
                    layer2(p - 2, 0)
                    if p == NP - 1:
                        variance2(p)
                    layer2(p - 2, 1)
            for p in range(NP - 2, NP):
                layer2(p, 0)
                layer2(p, 1)


def kernel(x, condB_t, L0_cond_W1, L0_cond_b1, L0_cond_W2, L0_cond_b2, L0_cond_Wsc, L0_cond_bsc, L0_cond_Wsh,
           L0_cond_bsh, L0_cond_gamma, L0_cond_beta, L0_cond_W_in, L0_cond_b_in, L0_cond_W_out, L0_cond_b_out):
    import concourse.bacc as bacc
    from concourse.bass_utils import run_bass_kernel_spmd

    def cols(a):
        return np.asarray(a).reshape(-1, P).T

    def features_first(a):
        return np.ascontiguousarray(np.asarray(a).T.reshape(C, P, S).transpose(1, 0, 2))

    half = E // 2
    freqs = np.exp(np.arange(half, dtype=np.float32) * np.float32(-math.log(10000.0) / (half - 1)))
    enc = np.zeros((P, N_ENC), np.float32)
    enc[:B, COL_EYE:] = np.eye(B, dtype=np.float32)
    enc[:, COL_FREQ] = np.tile(freqs, 2)
    enc[half:, COL_TURNS] = 0.25
    enc[half:, COL_PHASE] = math.pi / 2

    arrays = {
        "x": np.ascontiguousarray(np.asarray(x).reshape(NP, BP, S, C, P).transpose(0, 4, 3, 1, 2)),
        "t": np.ascontiguousarray(condB_t),
        "w1": np.ascontiguousarray(L0_cond_W1),
        "w2": np.ascontiguousarray(L0_cond_W2),
        "wsc": np.ascontiguousarray(L0_cond_Wsc),
        "wsh": np.ascontiguousarray(L0_cond_Wsh),
        "biases": np.ascontiguousarray(np.concatenate(
            [cols(a) for a in (L0_cond_b1, L0_cond_b2, L0_cond_bsc, L0_cond_bsh, L0_cond_b_in, L0_cond_b_out)], axis=1)),
        "gamma": features_first(L0_cond_gamma),
        "beta": features_first(L0_cond_beta),
        "w_in": np.ascontiguousarray(L0_cond_W_in),
        "w_out": np.ascontiguousarray(L0_cond_W_out),
        "enc": enc,
    }
    nc = bacc.Bacc("TRN2", target_bir_lowering=False, num_devices=1)
    args = {n: nc.dram_tensor(f"{n}_dram", a.shape, mybir.dt.from_np(a.dtype), kind="ExternalInput").ap()
            for n, a in arrays.items()}
    out = nc.dram_tensor("out_dram", (NP, P, C, BP, S), F32, kind="ExternalOutput").ap()
    build(nc, out=out, **args)
    r = run_bass_kernel_spmd(nc, [{f"{n}_dram": a for n, a in arrays.items()}], core_ids=[0])
    got = r.results[0]["out_dram"]
    return np.ascontiguousarray(got.transpose(0, 3, 4, 2, 1)).reshape(B, S, D)
```
